# Optimizing a Trainium2 kernel written in Bass

```python
import numpy as np
import jax
import jax.numpy as jnp

def _softmax(x, axis=-1):
    return jax.nn.softmax(x, axis=axis)

def _gelu(x):
    return jax.nn.gelu(x, approximate=True)

def _silu(x):
    return jax.nn.silu(x)

def _sigmoid(x):
    return jax.nn.sigmoid(x)

def _layernorm(x, axis=-1, eps=1e-05):
    m = jnp.mean(x, axis=axis, keepdims=True)
    v = jnp.var(x, axis=axis, keepdims=True)
    return (x - m) / jnp.sqrt(v + eps)

def _scatter_add(tgt, idx, src, axis=0):
    return tgt.at[idx].add(src)

def _segment_sum(src, seg, n):
    return jax.ops.segment_sum(src, seg, n)
kernel_name = 'mk_dlrm_tower_d1_rec_r8_455080'

def setup_inputs(seed: int=0):
    np.random.seed(seed)
    _w = jnp.asarray

    def _rec_inputs():
        import jax
        import jax.numpy as jnp
        _tk = jax.random.key(seed)
        dense_ctx = jax.random.normal(jax.random.fold_in(_tk, 190), (512, 16), jnp.float32)
        ids = jnp.stack([jax.random.randint(jax.random.fold_in(_tk, 200 + f), (512,), 0, v, jnp.int32) for f, v in enumerate([125000, 1250, 1000, 1250, 12500, 12500, 1000, 1000, 12500, 1000, 1000, 1250, 1000, 12500, 1000, 1000, 1000, 12500, 1000, 12500, 12500, 1250, 12500, 1250, 1000, 1000, 1000, 1250, 1250, 1000, 1250, 1250])], axis=1)
        tbl_0 = 0.05 * jax.random.normal(jax.random.fold_in(_tk, 500 + 0), (125000, 128), jnp.float32)
        tbl_1 = 0.05 * jax.random.normal(jax.random.fold_in(_tk, 500 + 1), (1250, 128), jnp.float32)
        tbl_2 = 0.05 * jax.random.normal(jax.random.fold_in(_tk, 500 + 2), (1000, 128), jnp.float32)
        tbl_3 = 0.05 * jax.random.normal(jax.random.fold_in(_tk, 500 + 3), (1250, 128), jnp.float32)
        tbl_4 = 0.05 * jax.random.normal(jax.random.fold_in(_tk, 500 + 4), (12500, 128), jnp.float32)
        tbl_5 = 0.05 * jax.random.normal(jax.random.fold_in(_tk, 500 + 5), (12500, 128), jnp.float32)
        tbl_6 = 0.05 * jax.random.normal(jax.random.fold_in(_tk, 500 + 6), (1000, 128), jnp.float32)
        tbl_7 = 0.05 * jax.random.normal(jax.random.fold_in(_tk, 500 + 7), (1000, 128), jnp.float32)
        tbl_8 = 0.05 * jax.random.normal(jax.random.fold_in(_tk, 500 + 8), (12500, 128), jnp.float32)
        tbl_9 = 0.05 * jax.random.normal(jax.random.fold_in(_tk, 500 + 9), (1000, 128), jnp.float32)
        tbl_10 = 0.05 * jax.random.normal(jax.random.fold_in(_tk, 500 + 10), (1000, 128), jnp.float32)
        tbl_11 = 0.05 * jax.random.normal(jax.random.fold_in(_tk, 500 + 11), (1250, 128), jnp.float32)
        tbl_12 = 0.05 * jax.random.normal(jax.random.fold_in(_tk, 500 + 12), (1000, 128), jnp.float32)
        tbl_13 = 0.05 * jax.random.normal(jax.random.fold_in(_tk, 500 + 13), (12500, 128), jnp.float32)
        tbl_14 = 0.05 * jax.random.normal(jax.random.fold_in(_tk, 500 + 14), (1000, 128), jnp.float32)
        tbl_15 = 0.05 * jax.random.normal(jax.random.fold_in(_tk, 500 + 15), (1000, 128), jnp.float32)
        tbl_16 = 0.05 * jax.random.normal(jax.random.fold_in(_tk, 500 + 16), (1000, 128), jnp.float32)
        tbl_17 = 0.05 * jax.random.normal(jax.random.fold_in(_tk, 500 + 17), (12500, 128), jnp.float32)
        tbl_18 = 0.05 * jax.random.normal(jax.random.fold_in(_tk, 500 + 18), (1000, 128), jnp.float32)
        tbl_19 = 0.05 * jax.random.normal(jax.random.fold_in(_tk, 500 + 19), (12500, 128), jnp.float32)
        tbl_20 = 0.05 * jax.random.normal(jax.random.fold_in(_tk, 500 + 20), (12500, 128), jnp.float32)
        tbl_21 = 0.05 * jax.random.normal(jax.random.fold_in(_tk, 500 + 21), (1250, 128), jnp.float32)
        tbl_22 = 0.05 * jax.random.normal(jax.random.fold_in(_tk, 500 + 22), (12500, 128), jnp.float32)
        tbl_23 = 0.05 * jax.random.normal(jax.random.fold_in(_tk, 500 + 23), (1250, 128), jnp.float32)
        tbl_24 = 0.05 * jax.random.normal(jax.random.fold_in(_tk, 500 + 24), (1000, 128), jnp.float32)
        tbl_25 = 0.05 * jax.random.normal(jax.random.fold_in(_tk, 500 + 25), (1000, 128), jnp.float32)
        tbl_26 = 0.05 * jax.random.normal(jax.random.fold_in(_tk, 500 + 26), (1000, 128), jnp.float32)
        tbl_27 = 0.05 * jax.random.normal(jax.random.fold_in(_tk, 500 + 27), (1250, 128), jnp.float32)
        tbl_28 = 0.05 * jax.random.normal(jax.random.fold_in(_tk, 500 + 28), (1250, 128), jnp.float32)
        tbl_29 = 0.05 * jax.random.normal(jax.random.fold_in(_tk, 500 + 29), (1000, 128), jnp.float32)
        tbl_30 = 0.05 * jax.random.normal(jax.random.fold_in(_tk, 500 + 30), (1250, 128), jnp.float32)
        tbl_31 = 0.05 * jax.random.normal(jax.random.fold_in(_tk, 500 + 31), (1250, 128), jnp.float32)
        _rk = jax.random.fold_in(_tk, 7)
        W_top1 = 0.0441942 * jax.random.normal(jax.random.fold_in(_tk, 801), (512, 512), jnp.float32)
        W_top2 = 0.0441942 * jax.random.normal(jax.random.fold_in(_tk, 802), (512, 256), jnp.float32)
        W_top3 = 0.0625 * jax.random.normal(jax.random.fold_in(_tk, 803), (256, 1), jnp.float32)
        b_top1 = jnp.zeros((512,), jnp.float32)
        b_top2 = jnp.zeros((256,), jnp.float32)
        return (dense_ctx, ids, tbl_0, tbl_1, tbl_2, tbl_3, tbl_4, tbl_5, tbl_6, tbl_7, tbl_8, tbl_9, tbl_10, tbl_11, tbl_12, tbl_13, tbl_14, tbl_15, tbl_16, tbl_17, tbl_18, tbl_19, tbl_20, tbl_21, tbl_22, tbl_23, tbl_24, tbl_25, tbl_26, tbl_27, tbl_28, tbl_29, tbl_30, tbl_31, W_top1, b_top1, W_top2, b_top2, W_top3)
    dense_ctx, ids, tbl_0, tbl_1, tbl_2, tbl_3, tbl_4, tbl_5, tbl_6, tbl_7, tbl_8, tbl_9, tbl_10, tbl_11, tbl_12, tbl_13, tbl_14, tbl_15, tbl_16, tbl_17, tbl_18, tbl_19, tbl_20, tbl_21, tbl_22, tbl_23, tbl_24, tbl_25, tbl_26, tbl_27, tbl_28, tbl_29, tbl_30, tbl_31, W_top1, b_top1, W_top2, b_top2, W_top3 = _rec_inputs()

    def _L0_rec_setup():
        import jax, jax.numpy as jnp
        import numpy as np
        N_FEATS = 32
        EMBED_D = 128
        BATCH = 2048
        SELF_INTERACTION = False
        key = jax.random.key(seed)
        x = jax.random.normal(key, (BATCH, N_FEATS, EMBED_D), dtype=jnp.float32)
        return {'x': x}
    _L0_rec_all = _L0_rec_setup()
    _L0_rec_in = {k: v for k, v in _L0_rec_all.items() if k in ()}
    del _L0_rec_all
    return {'dense_ctx': dense_ctx, 'ids': ids, 'tbl_0': tbl_0, 'tbl_1': tbl_1, 'tbl_2': tbl_2, 'tbl_3': tbl_3, 'tbl_4': tbl_4, 'tbl_5': tbl_5, 'tbl_6': tbl_6, 'tbl_7': tbl_7, 'tbl_8': tbl_8, 'tbl_9': tbl_9, 'tbl_10': tbl_10, 'tbl_11': tbl_11, 'tbl_12': tbl_12, 'tbl_13': tbl_13, 'tbl_14': tbl_14, 'tbl_15': tbl_15, 'tbl_16': tbl_16, 'tbl_17': tbl_17, 'tbl_18': tbl_18, 'tbl_19': tbl_19, 'tbl_20': tbl_20, 'tbl_21': tbl_21, 'tbl_22': tbl_22, 'tbl_23': tbl_23, 'tbl_24': tbl_24, 'tbl_25': tbl_25, 'tbl_26': tbl_26, 'tbl_27': tbl_27, 'tbl_28': tbl_28, 'tbl_29': tbl_29, 'tbl_30': tbl_30, 'tbl_31': tbl_31, 'W_top1': W_top1, 'b_top1': b_top1, 'W_top2': W_top2, 'b_top2': b_top2, 'W_top3': W_top3}

def reference(dense_ctx, ids, tbl_0, tbl_1, tbl_2, tbl_3, tbl_4, tbl_5, tbl_6, tbl_7, tbl_8, tbl_9, tbl_10, tbl_11, tbl_12, tbl_13, tbl_14, tbl_15, tbl_16, tbl_17, tbl_18, tbl_19, tbl_20, tbl_21, tbl_22, tbl_23, tbl_24, tbl_25, tbl_26, tbl_27, tbl_28, tbl_29, tbl_30, tbl_31, W_top1, b_top1, W_top2, b_top2, W_top3):
    import jax
    import jax.numpy as jnp

    def _L0_rec_ref(x):
        import jax, jax.numpy as jnp
        import numpy as np
        N_FEATS = 32
        EMBED_D = 128
        BATCH = 2048
        SELF_INTERACTION = False
        B, N, D = x.shape
        dot = jnp.einsum('bnd,bmd->bnm', x, x)
        k = 0 if SELF_INTERACTION else 1
        iu, ju = jnp.triu_indices(N, k=k)
        flat = dot[:, iu, ju]
        return flat
    e = jnp.stack([tbl_0[ids[:, 0]], tbl_1[ids[:, 1]], tbl_2[ids[:, 2]], tbl_3[ids[:, 3]], tbl_4[ids[:, 4]], tbl_5[ids[:, 5]], tbl_6[ids[:, 6]], tbl_7[ids[:, 7]], tbl_8[ids[:, 8]], tbl_9[ids[:, 9]], tbl_10[ids[:, 10]], tbl_11[ids[:, 11]], tbl_12[ids[:, 12]], tbl_13[ids[:, 13]], tbl_14[ids[:, 14]], tbl_15[ids[:, 15]], tbl_16[ids[:, 16]], tbl_17[ids[:, 17]], tbl_18[ids[:, 18]], tbl_19[ids[:, 19]], tbl_20[ids[:, 20]], tbl_21[ids[:, 21]], tbl_22[ids[:, 22]], tbl_23[ids[:, 23]], tbl_24[ids[:, 24]], tbl_25[ids[:, 25]], tbl_26[ids[:, 26]], tbl_27[ids[:, 27]], tbl_28[ids[:, 28]], tbl_29[ids[:, 29]], tbl_30[ids[:, 30]], tbl_31[ids[:, 31]]], axis=1)
    z = _L0_rec_ref(e)
    z = z.reshape(z.shape[0], -1)
    h = jnp.concatenate([z, dense_ctx], axis=1)
    h = jnp.maximum(h @ W_top1 + b_top1, 0.0)
    h = jnp.maximum(h @ W_top2 + b_top2, 0.0)
    y = h @ W_top3
    return y

_drawn_inputs = setup_inputs


def setup_inputs(seed=0):
    import zlib

    import numpy as np

    out = dict(_drawn_inputs(seed))
    spreads = {'b_top1': (0.0, 0.1), 'b_top2': (0.0, 0.1)}
    factors = {}
    for name, (base, spread) in spreads.items():
        noise = np.random.default_rng([zlib.crc32(name.encode()), seed]).standard_normal(out[name].shape)
        drawn = base * np.exp(spread * noise) if base else spread * noise
        out[name] = jnp.asarray(drawn.astype(out[name].dtype))
    for name, factor in factors.items():
        out[name] = (out[name] * factor).astype(out[name].dtype)
    return out
```

```python
from contextlib import ExitStack

import numpy as np

import concourse.bass as bass
from concourse import mybir

F32 = mybir.dt.float32
I32 = mybir.dt.int32
U32 = mybir.dt.uint32
ALU = mybir.AluOpType
ACT = mybir.ActivationFunctionType

P = 128
FEATS = 32
DIM = 128
QUAD = 32
NQ = P // QUAD
GROUP = P // FEATS
BANK = 512
SET = BANK // P
BLOCK = BANK // FEATS * GROUP
GATHERS = BLOCK // GROUP
SETS = GATHERS // SET
CHUNKS = FEATS // NQ
UNROLL = 2
TURN = UNROLL * BLOCK


def build_tower(nc, table, ids, row_base, dense, w1, b1, w2, b2, w3, out):
    n_batch = out.shape[0]
    n_dense = dense.shape[0]
    n_h1, n_h2 = w2.shape
    M1, M2 = n_h1 // P, n_h2 // P
    turns = n_batch // TURN

    with ExitStack() as ctx:
        def sb(name, shape, dt=F32):
            return ctx.enter_context(nc.sbuf_tensor(name, shape, dt))

        def psum(name, shape):
            return ctx.enter_context(nc.psum_tensor(name, shape, F32))

        def sem(name):
            return ctx.enter_context(nc.semaphore(name))

        ids_sb = sb("ids_sb", [P, (turns + 1) * UNROLL * GATHERS], I32)
        base_sb = sb("base_sb", [P, 1])
        row_idx = sb("row_idx", [P, UNROLL, GATHERS], I32)
        rows = sb("rows", [P, UNROLL * GATHERS, DIM])
        emb_t = sb("emb_t", [P, UNROLL, GATHERS, P])
        identity = sb("identity", [P, P])
        pairs = sb("pairs", [P, CHUNKS, n_batch])
        w1_sb = sb("w1_sb", [P, CHUNKS, n_h1])
        w2_sb = sb("w2_sb", [P, M1, n_h2])
        w3_sb = sb("w3_sb", [P, M2])
        b1_sb = sb("b1_sb", [P, M1])
        b2_sb = sb("b2_sb", [P, M2])
        h1 = sb("h1", [P, M1, TURN])
        h2 = sb("h2", [P, M2, TURN])
        y = sb("y", [1, n_batch])

        turned = [psum(f"turned{i}", [P, SET, P]) for i in range(2)]
        gram = [psum(f"gram{i}", [P, GATHERS, FEATS]) for i in range(UNROLL)]
        h1_ps = psum("h1_ps", [P, M1, TURN])
        h2_ps = psum("h2_ps", [P, M2, TURN])
        y_ps = psum("y_ps", [1, TURN])

        ids_in = sem("ids_in")
        base_in = sem("base_in")
        ids_padded = sem("ids_padded")
        dense_in = sem("dense_in")
        weights_in = sem("weights_in")
        zeroed = sem("zeroed")
        identity_ready = sem("identity_ready")
        dense_cleared = sem("dense_cleared")
        idx_ready = sem("idx_ready")
        gather_waits = sem("gather_waits")
        gathered = [sem(f"gathered{i}") for i in range(UNROLL * SETS)]
        transposed = sem("transposed")
        even_copied = sem("even_copied")
        odd_copied = sem("odd_copied")
        gram_ready = sem("gram_ready")
        pairs_low = sem("pairs_low")
        pairs_high = sem("pairs_high")
        h1_done = sem("h1_done")
        h1_ready = sem("h1_ready")
        h2_done = sem("h2_done")
        h2_ready = sem("h2_ready")
        y_done = sem("y_done")
        y_ready = sem("y_ready")
        stored = sem("stored")

        block = ctx.enter_context(nc.Block())
        n_weights = 5

        @block.sync
        def _(sp):
            sp.dma_start(ids_sb[:, 0:turns * UNROLL * GATHERS], ids).then_inc(ids_in, 16)
            sp.dma_start(w1_sb[:], w1.rearrange("p (c n) -> p c n", c=CHUNKS)).then_inc(weights_in, 16)
            sp.dma_start(w2_sb[:], w2.rearrange("(k p) n -> p k n", p=P)).then_inc(weights_in, 16)
            sp.dma_start(w3_sb[:], w3).then_inc(weights_in, 16)
            sp.dma_start(b1_sb[:], b1).then_inc(weights_in, 16)
            sp.dma_start(b2_sb[:], b2).then_inc(weights_in, 16)
            sp.wait_ge(dense_cleared, 1)
            sp.dma_start(pairs[0:n_dense, 0, :], dense).then_inc(dense_in, 16)
            sp.wait_ge(y_ready, turns)
            sp.dma_start(out.rearrange("b o -> o b"), y[:]).then_inc(stored, 16)
            sp.wait_ge(stored, 16)

        @block.gpsimd
        def _(pool):
            nc.gpsimd.memset(identity[:], 0.0).then_inc(zeroed, 1)
            pool.wait_ge(zeroed, 1)
            nc.gpsimd.affine_select(out=identity[:], in_=identity[:], compare_op=ALU.not_equal, fill=1.0, base=0,
                                    pattern=[[-1, P]], channel_multiplier=1).then_inc(identity_ready, 1)

            def wait(signal, value):
                pool.wait_ge(signal, value)
                pool.sem_inc(gather_waits, 1)

            with pool.Fori(0, turns) as t:
                for u in range(UNROLL):
                    wait(idx_ready, t * UNROLL + (u + 1))
                    for k in range(GATHERS):
                        slot = u * GATHERS + k
                        if k % SET == 0:
                            wait(transposed, t * (UNROLL * SETS) + (u * SETS + k // SET + 1))
                        pool.indirect_dma_start(
                            rows[:, slot, :], None, table,
                            bass.IndirectOffsetOnAxis(row_idx[:, u, k:k + 1].bitcast(U32), 0),
                        ).then_inc(gathered[slot // SET], 16)

        def copy_set(eng, copy, u, n, done, t):
            eng.wait_ge(transposed, t * (UNROLL * SETS) + (UNROLL * SETS + u * SETS + n + 1))
            copy(emb_t[:, u, n * SET:(n + 1) * SET, :], turned[n % 2][:]).then_inc(done, 1)

        def move_pairs(copy, u, samples, t, done):
            start = t * TURN + u * BLOCK
            for s in samples:
                for q in range(NQ):
                    c0 = 1 if q == 0 else 0
                    src = gram[u][s * QUAD:(s + 1) * QUAD, :, :].rearrange("p g (c q) -> p c g q", q=NQ)
                    dst = pairs[q * QUAD:(q + 1) * QUAD, c0:, bass.ds(start, BLOCK)]
                    dst = dst.rearrange("p c (g s) -> p c g s", s=GROUP)
                    last = copy(dst[:, :, :, s], src[:, c0:, :, q])
            last.then_inc(done, 1)

        @block.vector
        def _(dve):
            nc.vector.memset(pairs[0:QUAD, 0, :], 0.0).then_inc(dense_cleared, 1)
            nc.vector.memset(ids_sb[:, turns * UNROLL * GATHERS:], 0.0).then_inc(ids_padded, 1)
            dve.wait_ge(ids_padded, 1)
            dve.wait_ge(ids_in, 16)
            dve.wait_ge(base_in, 16)

            def number_rows(turn, u):
                nc.vector.tensor_scalar(row_idx[:, u, :],
                                        ids_sb[:, bass.ds(turn * (UNROLL * GATHERS) + u * GATHERS, GATHERS)],
                                        base_sb[:, 0:1], None, ALU.add).then_inc(idx_ready, 1)

            for u in range(UNROLL):
                number_rows(0, u)
            with dve.Fori(0, turns) as t:
                for u in range(UNROLL):
                    for n in range(0, SETS, 2):
                        copy_set(dve, nc.vector.tensor_copy, u, n, even_copied, t)
                    dve.wait_ge(transposed, t * (UNROLL * SETS) + (UNROLL * SETS + (u + 1) * SETS))
                    number_rows(t + 1, u)
                    dve.wait_ge(gram_ready, t * UNROLL + (u + 1))
                    move_pairs(nc.vector.tensor_copy, u, range(GROUP // 2, GROUP), t, pairs_high)

        @block.scalar
        def _(act):
            act.dma_start(base_sb[:], row_base).then_inc(base_in, 16)
            with act.Fori(0, turns) as t:
                for u in range(UNROLL):
                    for n in range(1, SETS, 2):
                        copy_set(act, nc.scalar.copy, u, n, odd_copied, t)
                    act.wait_ge(gram_ready, t * UNROLL + (u + 1))
                    move_pairs(nc.scalar.copy, u, range(GROUP // 2), t, pairs_low)
                act.wait_ge(weights_in, 16 * n_weights)
                act.wait_ge(h1_done, t + 1)
                for m in range(M1):
                    last = nc.scalar.activation(h1[:, m, :], h1_ps[:, m, :], ACT.Relu, bias=b1_sb[:, m:m + 1])
                last.then_inc(h1_ready, 1)
                act.wait_ge(h2_done, t + 1)
                for m in range(M2):
                    last = nc.scalar.activation(h2[:, m, :], h2_ps[:, m, :], ACT.Relu, bias=b2_sb[:, m:m + 1])
                last.then_inc(h2_ready, 1)
                act.wait_ge(y_done, t + 1)
                nc.scalar.copy(y[:, bass.ds(t * TURN, TURN)], y_ps[:]).then_inc(y_ready, 1)

        @block.tensor
        def _(pe):
            pe.sem_inc(transposed, UNROLL * SETS)
            pe.wait_ge(identity_ready, 1)
            with pe.Fori(0, turns) as t:
                for u in range(UNROLL):
                    def transpose_set(n):
                        pe.wait_ge(gathered[u * SETS + n], t * (16 * SET) + 16 * SET)
                        if n >= 2:
                            pe.wait_ge((even_copied, odd_copied)[n % 2], t * (UNROLL * SETS // 2) + (u * SETS + n) // 2)
                        for k in range(SET):
                            last = nc.tensor.transpose(turned[n % 2][:, k, :], rows[:, u * GATHERS + n * SET + k, :],
                                                       identity[:])
                        last.then_inc(transposed, 1)

                    def gram_set(n):
                        pe.wait_ge((even_copied, odd_copied)[n % 2],
                                   t * (UNROLL * SETS // 2) + (u * SETS + n) // 2 + 1)
                        for k in range(n * SET, (n + 1) * SET):
                            for s in range(GROUP):
                                x = emb_t[:, u, k, s * FEATS:(s + 1) * FEATS]
                                last = nc.tensor.matmul(gram[u][s * QUAD:(s + 1) * QUAD, k, :], x, x,
                                                        start=True, stop=True)
                        return last

                    transpose_set(0)
                    for n in range(1, SETS):
                        transpose_set(n)
                        gram_set(n - 1)
                    gram_set(SETS - 1).then_inc(gram_ready, 1)
                pe.wait_ge(weights_in, 16 * n_weights)
                pe.wait_ge(dense_in, 16)
                pe.wait_ge(pairs_low, t * UNROLL + UNROLL)
                pe.wait_ge(pairs_high, t * UNROLL + UNROLL)
                for m in range(M1):
                    for c in range(CHUNKS):
                        last = nc.tensor.matmul(h1_ps[:, m, :], w1_sb[:, c, m * P:(m + 1) * P],
                                                pairs[:, c, bass.ds(t * TURN, TURN)],
                                                start=(c == 0), stop=(c == CHUNKS - 1))
                last.then_inc(h1_done, 1)
                pe.wait_ge(h1_ready, t + 1)
                for m in range(M2):
                    for k in range(M1):
                        last = nc.tensor.matmul(h2_ps[:, m, :], w2_sb[:, k, m * P:(m + 1) * P], h1[:, k, :],
                                                start=(k == 0), stop=(k == M1 - 1))
                last.then_inc(h2_done, 1)
                pe.wait_ge(h2_ready, t + 1)
                for k in range(M2):
                    last = nc.tensor.matmul(y_ps[:], w3_sb[:, k:k + 1], h2[:, k, :],
                                            start=(k == 0), stop=(k == M2 - 1))
                last.then_inc(y_done, 1)


def kernel(**inputs):
    import concourse.bacc as bacc
    from concourse.bass_utils import run_bass_kernel_spmd

    a = {name: np.asarray(value) for name, value in inputs.items()}
    tables = [a[f"tbl_{f}"] for f in range(FEATS)]
    first_row = np.cumsum([0] + [t.shape[0] for t in tables[:-1]])

    w1 = a["W_top1"]
    n_pairs = FEATS * (FEATS - 1) // 2
    low, high = np.triu_indices(FEATS, k=1)
    w1_placed = np.zeros((NQ, QUAD, CHUNKS, w1.shape[1]), w1.dtype)
    w1_placed[high % NQ, low, high // NQ] = w1[:n_pairs]
    w1_placed[0, :w1.shape[0] - n_pairs, 0] = w1[n_pairs:]

    arrays = {
        "table_dram": np.concatenate(tables),
        "ids_dram": np.ascontiguousarray(a["ids"].reshape(-1, P).T),
        "row_base_dram": np.tile(first_row, GROUP).astype(np.float32).reshape(P, 1),
        "dense_dram": np.ascontiguousarray(a["dense_ctx"].T),
        "w1_dram": w1_placed.reshape(P, -1),
        "b1_dram": np.ascontiguousarray(a["b_top1"].reshape(-1, P).T),
        "w2_dram": a["W_top2"],
        "b2_dram": np.ascontiguousarray(a["b_top2"].reshape(-1, P).T),
        "w3_dram": np.ascontiguousarray(a["W_top3"].reshape(-1, P).T),
    }
    nc = bacc.Bacc("TRN2", target_bir_lowering=False, num_devices=1)
    args = [nc.dram_tensor(name, v.shape, mybir.dt.from_np(v.dtype), kind="ExternalInput").ap()
            for name, v in arrays.items()]
    out = nc.dram_tensor("out_dram", (a["ids"].shape[0], 1), F32, kind="ExternalOutput").ap()
    build_tower(nc, *args, out)
    result = run_bass_kernel_spmd(nc, [arrays], core_ids=[0])
    return result.results[0]["out_dram"]
```

```python
from contextlib import ExitStack

import numpy as np

import concourse.bass as bass
from concourse import mybir

F32 = mybir.dt.float32
BF16 = mybir.dt.bfloat16
F16 = mybir.dt.float16
I32 = mybir.dt.int32
U32 = mybir.dt.uint32
ALU = mybir.AluOpType
ACT = mybir.ActivationFunctionType

P = 128
FEATS = 32
HOT = 8
COLD = FEATS - HOT
DIM = 128
HOT_CHUNKS = 8
HOT_BUFS = 4
HOT_BANKS = 2
BANKS = 4
QUAD = 32
NQ = P // QUAD
BANK = 512
BLOCK = NQ * BANK // FEATS
PER_GATHER = P // BLOCK
GATHERS = COLD // PER_GATHER
SET = BANK // P
SETS = GATHERS // SET
SET_FEATS = SET * PER_GATHER
CHUNKS = FEATS // NQ
UNIT = 2 * BLOCK
BLOCKS = 4
TURN = BLOCKS * BLOCK
UNITS = TURN // UNIT
SETS_T = BLOCKS * SETS
assert GATHERS % SET == 0 and SETS_T % BANKS == 0


def build_tower(nc, table, ids, first_rows, hot_tables, hot_ids, row_numbers, dense, w1, b1, w2, b2, w3, out):
    n_batch = out.shape[0]
    n_dense = dense.shape[0]
    n_h1, n_h2 = w2.shape
    M1, M2 = n_h1 // P, n_h2 // P
    turns = n_batch // TURN
    n_gathers = ids.shape[1]
    hot_turns = HOT // HOT_BUFS

    with ExitStack() as ctx:
        def sb(name, shape, dt=F32):
            return ctx.enter_context(nc.sbuf_tensor(name, shape, dt))

        def psum(name, shape):
            return ctx.enter_context(nc.psum_tensor(name, shape, F32))

        def sem(name):
            return ctx.enter_context(nc.semaphore(name))

        ids_sb = sb("ids_sb", [P, n_gathers], I32)
        first_sb = sb("first_sb", [P, n_gathers], I32)
        all_rows = sb("all_rows", [P, n_gathers], I32)
        row_idx = sb("row_idx", [P, BLOCKS, GATHERS], I32)
        rows = sb("rows", [P, BLOCKS * GATHERS, DIM])
        identity = sb("identity", [P, P])
        numbers_sb = sb("numbers_sb", [P, HOT_CHUNKS])
        hot_id = sb("hot_id", [P, HOT, n_batch], I32)
        hot_id_16 = sb("hot_id_16", [P, HOT, n_batch], F16)
        one_hot = [sb(f"one_hot{i}", [P, HOT_CHUNKS, n_batch], BF16) for i in range(HOT_BUFS)]
        whole = [sb(f"whole{i}", [P, HOT_CHUNKS, DIM]) for i in range(HOT_BUFS)]
        rest = [sb(f"rest{i}", [P, HOT_CHUNKS, DIM]) for i in range(HOT_BUFS)]
        low = [sb(f"low{i}", [P, HOT_CHUNKS, DIM], BF16) for i in range(HOT_BUFS)]
        hot_t = sb("hot_t", [P, HOT, n_batch])
        emb_t = [sb(f"emb_t{i}", [P, BLOCK, FEATS]) for i in range(2)]
        pairs = sb("pairs", [P, CHUNKS, n_batch])
        w1_sb = sb("w1_sb", [P, CHUNKS, n_h1])
        w2_sb = sb("w2_sb", [P, M1, n_h2])
        w3_sb = sb("w3_sb", [P, M2])
        b1_sb = sb("b1_sb", [P, M1])
        b2_sb = sb("b2_sb", [P, M2])
        h1 = sb("h1", [P, M1, UNIT])
        h2 = sb("h2", [P, M2, UNIT])
        y = sb("y", [1, n_batch])

        turned = [psum(f"turned{i}", [P, SET_FEATS, BLOCK]) for i in range(BANKS)]
        hot_ps = [turned[BANKS - HOT_BANKS + i][:].rearrange("p f s -> p (f s)") for i in range(HOT_BANKS)]
        gram = [psum(f"gram{i}", [P, BLOCK // NQ, FEATS]) for i in range(2)]
        h1_ps = psum("h1_ps", [P, M1, UNIT])
        h2y_ps = psum("h2y_ps", [P, M2 + 1, UNIT])
        h2_ps = h2y_ps[:, 0:M2, :]
        y_ps = h2y_ps[0:1, M2, :]

        def upper(x):
            return x.bitcast(BF16).rearrange("p c (d h) -> p c d h", h=2)[:, :, :, 1]

        ids_in = sem("ids_in")
        numbers_in = sem("numbers_in")
        dense_in = sem("dense_in")
        weights_in = sem("weights_in")
        n_weights = 5
        table_in = [sem(f"table_in{i}") for i in range(HOT_BUFS)]
        hot_id_in = [sem(f"hot_id_in{i}") for i in range(HOT)]
        ids_16_ready = sem("ids_16_ready")
        one_hot_ready = sem("one_hot_ready")
        rest_ready = sem("rest_ready")
        low_ready = sem("low_ready")
        hot_done = sem("hot_done")
        hot_banks = sem("hot_banks")
        zeroed = sem("zeroed")
        identity_ready = sem("identity_ready")
        dense_cleared = sem("dense_cleared")
        rows_known = sem("rows_known")
        idx_ready = sem("idx_ready")
        gather_waits = sem("gather_waits")
        gathered = [sem(f"gathered{i}") for i in range(SETS_T)]
        transposed = sem("transposed")
        copied = [sem("even_copied"), sem("odd_copied")]
        hot_placed = sem("hot_placed")
        gram_ready = sem("gram_ready")
        pairs_low = sem("pairs_low")
        pairs_high = sem("pairs_high")
        h1_done = sem("h1_done")
        h1_ready = sem("h1_ready")
        h2_done = sem("h2_done")
        h2_ready = sem("h2_ready")
        y_done = sem("y_done")
        y_ready = sem("y_ready")
        stored = sem("stored")

        block = ctx.enter_context(nc.Block())

        @block.sync
        def _(sp):
            def load_hot(i, w):
                sp.dma_start(whole[w][:], hot_tables[bass.ds(i, 1), :, :, :].rearrange("i p c d -> (i p) c d")
                             ).then_inc(table_in[w], 16)

            def load_hot_ids(i):
                sp.dma_start(hot_id[:, i, :], hot_ids[i:i + 1, :].broadcast_to([P, n_batch])
                             ).then_inc(hot_id_in[i], 16)

            sp.dma_start(ids_sb[:], ids).then_inc(ids_in, 16)
            sp.dma_start(first_sb[:], first_rows).then_inc(ids_in, 16)
            for w in range(HOT_BUFS):
                load_hot_ids(w)
                load_hot(w, w)
            for i in range(HOT_BUFS, HOT):
                load_hot_ids(i)
            sp.dma_start(w1_sb[:], w1.rearrange("p (c n) -> p c n", c=CHUNKS)).then_inc(weights_in, 16)
            sp.dma_start(w2_sb[:], w2.rearrange("(k p) n -> p k n", p=P)).then_inc(weights_in, 16)
            with sp.Fori(1, hot_turns) as j:
                for w in range(HOT_BUFS):
                    sp.wait_ge(hot_done, j * HOT_BUFS + (w + 1 - HOT_BUFS))
                    load_hot(j * HOT_BUFS + w, w)
            sp.wait_ge(y_ready, n_batch // UNIT)
            sp.dma_start(out.rearrange("b o -> o b"), y[:]).then_inc(stored, 16)
            sp.wait_ge(stored, 16)

        @block.gpsimd
        def _(pool):
            nc.gpsimd.memset(identity[:], 0.0).then_inc(zeroed, 1)
            pool.wait_ge(zeroed, 1)
            nc.gpsimd.affine_select(out=identity[:], in_=identity[:], compare_op=ALU.not_equal, fill=1.0, base=0,
                                    pattern=[[-1, P]], channel_multiplier=1).then_inc(identity_ready, 1)

            def wait(signal, value):
                pool.wait_ge(signal, value)
                pool.sem_inc(gather_waits, 1)

            def gather_turn(t, first):
                for u in range(BLOCKS):
                    wait(idx_ready, t * BLOCKS + (u + 1))
                    for k in range(GATHERS):
                        at = u * SETS + k // SET
                        if k % SET == 0 and not first:
                            wait(transposed, t * SETS_T + (at + 1 - SETS_T))
                        pool.indirect_dma_start(
                            rows[:, u * GATHERS + k, :], None, table,
                            bass.IndirectOffsetOnAxis(row_idx[:, u, k:k + 1].bitcast(U32), 0),
                        ).then_inc(gathered[at], 16)

            gather_turn(0, True)
            with pool.Fori(1, turns) as t:
                gather_turn(t, False)

        def copy_sets(eng, copy, parity, t, u):
            for n in range(SETS):
                at = u * SETS + n
                if at % 2 != parity:
                    continue
                eng.wait_ge(transposed, t * SETS_T + (at + 1))
                dst = emb_t[u % 2][:, :, n * SET_FEATS:(n + 1) * SET_FEATS].rearrange("p s f -> p f s")
                copy(dst, turned[at % BANKS][:]).then_inc(copied[parity], 1)

        def move_pairs(eng, copy, samples, t, u, done):
            eng.wait_ge(gram_ready, t * BLOCKS + (u + 1))
            start = t * TURN + u * BLOCK
            for s in samples:
                for q in range(NQ):
                    c0 = 1 if q == 0 else 0
                    src = gram[u % 2][s * QUAD:(s + 1) * QUAD, :, :].rearrange("p g (c q) -> p c g q", q=NQ)
                    dst = pairs[q * QUAD:(q + 1) * QUAD, c0:, bass.ds(start, BLOCK)]
                    dst = dst.rearrange("p c (g s) -> p c g s", s=NQ)
                    last = copy(dst[:, :, :, s], src[:, c0:, :, q])
            last.then_inc(done, 1)

        @block.vector
        def _(dve):
            nc.vector.memset(pairs[0:QUAD, 0, :], 0.0).then_inc(dense_cleared, 1)
            dve.wait_ge(ids_in, 32)
            nc.vector.tensor_tensor(all_rows[:], ids_sb[:], first_sb[:], ALU.add).then_inc(rows_known, 1)
            dve.wait_ge(rows_known, 1)

            def number_rows(t, u):
                nc.vector.tensor_copy(row_idx[:, u, :], all_rows[:, bass.ds(t * (BLOCKS * GATHERS) + u * GATHERS, GATHERS)]
                                      ).then_inc(idx_ready, 1)

            for u in range(BLOCKS):
                number_rows(0, u)

            dve.wait_ge(numbers_in, 16)
            with dve.Fori(0, hot_turns) as j:
                for w in range(HOT_BUFS):
                    dve.wait_ge(ids_16_ready, j * HOT_BUFS + (w + 1))
                    dve.wait_ge(table_in[w], j * 16 + 16)
                    for c in range(HOT_CHUNKS):
                        last = nc.vector.tensor_scalar(
                            one_hot[w][:, c, :], hot_id_16[:, bass.ds(j * HOT_BUFS + w, 1), :].rearrange("p h b -> p (h b)"),
                            numbers_sb[:, c:c + 1], None, ALU.is_equal)
                    last.then_inc(one_hot_ready, 1)
                    nc.vector.tensor_tensor(rest[w][:], whole[w][:], upper(whole[w][:]), ALU.subtract
                                            ).then_inc(rest_ready, 1)
                    dve.wait_ge(rest_ready, j * HOT_BUFS + (w + 1))
                    nc.vector.tensor_tensor(low[w][:], rest[w][:], upper(rest[w][:]), ALU.subtract
                                            ).then_inc(low_ready, 1)

            def copy_block(t, u):
                copy_sets(dve, nc.vector.tensor_copy, 0, t, u)

            def move_block(t, u):
                move_pairs(dve, nc.vector.tensor_copy, range(NQ // 2, NQ), t, u, pairs_high)

            def turn(t, last):
                for u in range(BLOCKS):
                    copy_block(t, u)
                    if not last:
                        dve.wait_ge(transposed, t * SETS_T + (u + 1) * SETS)
                        number_rows(t + 1, u)
                    move_block(t, u)

            with dve.Fori(0, turns - 1) as t:
                turn(t, False)
            turn(turns - 1, True)

        @block.scalar
        def _(act):
            act.dma_start(numbers_sb[:], row_numbers).then_inc(numbers_in, 16)
            act.dma_start(w3_sb[:], w3).then_inc(weights_in, 16)
            act.dma_start(b1_sb[:], b1).then_inc(weights_in, 16)
            act.dma_start(b2_sb[:], b2).then_inc(weights_in, 16)
            act.wait_ge(dense_cleared, 1)
            act.dma_start(pairs[0:n_dense, 0, :], dense).then_inc(dense_in, 16)

            for i in range(HOT):
                act.wait_ge(hot_id_in[i], 16)
                nc.scalar.copy(hot_id_16[:, i, :], hot_id[:, i, :]).then_inc(ids_16_ready, 1)
            with act.Fori(0, hot_turns) as j:
                for w in range(HOT_BUFS):
                    act.wait_ge(hot_done, j * HOT_BUFS + (w + 1))
                    nc.scalar.copy(hot_t[:, bass.ds(j * HOT_BUFS + w, 1), :].rearrange("p h b -> p (h b)"),
                                   hot_ps[w % HOT_BANKS]).then_inc(hot_banks, 1)
            act.wait_ge(hot_banks, HOT_BANKS + HOT)
            act.wait_ge(weights_in, 16 * n_weights)

            def fill_block(t, u):
                nc.scalar.copy(emb_t[u % 2][:, :, COLD:].rearrange("p s f -> p f s"),
                               hot_t[:, :, bass.ds(t * TURN + u * BLOCK, BLOCK)]).then_inc(hot_placed, 1)
                copy_sets(act, nc.scalar.copy, 1, t, u)

            def move_block(t, u):
                move_pairs(act, nc.scalar.copy, range(NQ // 2), t, u, pairs_low)

            def hidden(dst, src, bias, tiles, t, v, done, ready):
                act.wait_ge(done, t * UNITS + (v + 1))
                for m in range(tiles):
                    last = nc.scalar.activation(dst[:, m, :], src[:, m, :], ACT.Relu, bias=bias[:, m:m + 1])
                last.then_inc(ready, 1)

            def hidden1(t, v):
                hidden(h1, h1_ps, b1_sb, M1, t, v, h1_done, h1_ready)

            def hidden2(t, v):
                hidden(h2, h2_ps, b2_sb, M2, t, v, h2_done, h2_ready)

            def result(t, v):
                act.wait_ge(y_done, t * UNITS + (v + 1))
                nc.scalar.copy(y[:, bass.ds(t * TURN + v * UNIT, UNIT)], y_ps).then_inc(y_ready, 1)

            def turn(t, first):
                for v in range(UNITS):
                    before = (t, v - 1) if v else (t - 1, UNITS - 1)
                    fill_block(t, 2 * v)
                    if v or not first:
                        hidden1(*before)
                    move_block(t, 2 * v)
                    if v or not first:
                        hidden2(*before)
                    fill_block(t, 2 * v + 1)
                    if v or not first:
                        result(*before)
                    move_block(t, 2 * v + 1)

            turn(0, True)
            with act.Fori(1, turns) as t:
                turn(t, False)
            hidden1(turns - 1, UNITS - 1)
            hidden2(turns - 1, UNITS - 1)
            result(turns - 1, UNITS - 1)

        @block.tensor
        def _(pe):
            pe.sem_inc(hot_banks, HOT_BANKS)
            with pe.Fori(0, hot_turns) as j:
                for w in range(HOT_BUFS):
                    pe.wait_ge(hot_banks, j * HOT_BUFS + (w + 1))
                    parts = [(upper(whole[w][:]), one_hot_ready), (upper(rest[w][:]), rest_ready),
                             (low[w][:], low_ready)]
                    for n, (part, ready) in enumerate(parts):
                        pe.wait_ge(ready, j * HOT_BUFS + (w + 1))
                        for c in range(HOT_CHUNKS):
                            last = nc.tensor.matmul(hot_ps[w % HOT_BANKS], part[:, c, :], one_hot[w][:, c, :],
                                                    start=(n == 0 and c == 0),
                                                    stop=(n == len(parts) - 1 and c == HOT_CHUNKS - 1))
                    last.then_inc(hot_done, 1)

            def transpose_block(t, u, first):
                for n in range(SETS):
                    at = u * SETS + n
                    pe.wait_ge(gathered[at], t * (16 * SET) + 16 * SET)
                    if at >= BANKS or not first:
                        pe.wait_ge(copied[at % 2], t * (SETS_T // 2) + (at // 2 + 1 - BANKS // 2))
                    for k in range(SET):
                        last = nc.tensor.transpose(
                            turned[at % BANKS][:, k * PER_GATHER:(k + 1) * PER_GATHER, :],
                            rows[:, u * GATHERS + n * SET + k, :], identity[:])
                    last.then_inc(transposed, 1)

            def gram_block(t, u):
                sets = (u + 1) * SETS
                pe.wait_ge(copied[0], t * (SETS_T // 2) + (sets + 1) // 2)
                pe.wait_ge(copied[1], t * (SETS_T // 2) + sets // 2)
                pe.wait_ge(hot_placed, t * BLOCKS + (u + 1))
                for g in range(BLOCK // NQ):
                    for s in range(NQ):
                        x = emb_t[u % 2][:, g * NQ + s, :]
                        last = nc.tensor.matmul(gram[u % 2][s * QUAD:(s + 1) * QUAD, g, :], x, x,
                                                start=True, stop=True)
                last.then_inc(gram_ready, 1)

            def layer1(t, v):
                pe.wait_ge(pairs_low, t * BLOCKS + (2 * v + 2))
                pe.wait_ge(pairs_high, t * BLOCKS + (2 * v + 2))
                for m in range(M1):
                    for c in range(CHUNKS):
                        last = nc.tensor.matmul(h1_ps[:, m, :], w1_sb[:, c, m * P:(m + 1) * P],
                                                pairs[:, c, bass.ds(t * TURN + v * UNIT, UNIT)],
                                                start=(c == 0), stop=(c == CHUNKS - 1))
                last.then_inc(h1_done, 1)

            def layer2(t, v):
                pe.wait_ge(h1_ready, t * UNITS + (v + 1))
                for m in range(M2):
                    for k in range(M1):
                        last = nc.tensor.matmul(h2_ps[:, m, :], w2_sb[:, k, m * P:(m + 1) * P], h1[:, k, :],
                                                start=(k == 0), stop=(k == M1 - 1))
                last.then_inc(h2_done, 1)

            def layer3(t, v):
                pe.wait_ge(h2_ready, t * UNITS + (v + 1))
                for k in range(M2):
                    last = nc.tensor.matmul(y_ps, w3_sb[:, k:k + 1], h2[:, k, :],
                                            start=(k == 0), stop=(k == M2 - 1))
                last.then_inc(y_done, 1)

            def turn(t, first):
                for v in range(UNITS):
                    before = (t, v - 1) if v else (t - 1, UNITS - 1)
                    transpose_block(t, 2 * v, first)
                    if v or not first:
                        layer1(*before)
                    gram_block(t, 2 * v)
                    if v or not first:
                        layer2(*before)
                    transpose_block(t, 2 * v + 1, first)
                    if v or not first:
                        layer3(*before)
                    gram_block(t, 2 * v + 1)

            pe.wait_ge(identity_ready, 1)
            pe.wait_ge(weights_in, 16 * n_weights)
            pe.wait_ge(dense_in, 16)
            pe.wait_ge(hot_banks, HOT_BANKS + HOT)
            turn(0, True)
            with pe.Fori(1, turns) as t:
                turn(t, False)
            layer1(turns - 1, UNITS - 1)
            layer2(turns - 1, UNITS - 1)
            layer3(turns - 1, UNITS - 1)


def kernel(**inputs):
    import concourse.bacc as bacc
    from concourse.bass_utils import run_bass_kernel_spmd

    a = {name: np.asarray(value) for name, value in inputs.items()}
    tables = [a[f"tbl_{f}"] for f in range(FEATS)]
    n_batch = a["ids"].shape[0]
    blocks = n_batch // BLOCK

    small = [f for f in range(FEATS) if tables[f].shape[0] <= 1000]
    hot = small[-HOT:]
    cold = [f for f in range(FEATS) if f not in hot]
    slots = np.array(cold + hot)

    first_row = np.cumsum([0] + [tables[f].shape[0] for f in cold[:-1]]).astype(np.int32)
    by_gather = (PER_GATHER, BLOCK, blocks, GATHERS)
    ids = a["ids"][:, cold].reshape(blocks, BLOCK, GATHERS, PER_GATHER).transpose(3, 1, 0, 2)
    first = np.broadcast_to(first_row.reshape(GATHERS, PER_GATHER).T[:, None, None, :], by_gather)

    hot_tables = np.zeros((HOT, HOT_CHUNKS * P, DIM), tables[0].dtype)
    for n, f in enumerate(hot):
        hot_tables[n, :tables[f].shape[0]] = tables[f]

    w1 = a["W_top1"]
    i, j = np.triu_indices(FEATS, k=1)
    n_pairs = len(i)
    row_of = np.zeros((FEATS, FEATS), np.int64)
    row_of[i, j] = row_of[j, i] = np.arange(n_pairs)
    w1_placed = np.zeros((NQ, QUAD, CHUNKS, w1.shape[1]), w1.dtype)
    w1_placed[j % NQ, i, j // NQ] = w1[row_of[slots[i], slots[j]]]
    w1_placed[0, :w1.shape[0] - n_pairs, 0] = w1[n_pairs:]

    arrays = {
        "table_dram": np.concatenate([tables[f] for f in cold]),
        "ids_dram": np.ascontiguousarray(ids).reshape(P, -1),
        "first_rows_dram": np.ascontiguousarray(first).reshape(P, -1),
        "hot_tables_dram": hot_tables.reshape(HOT, P, HOT_CHUNKS, DIM),
        "hot_ids_dram": np.ascontiguousarray(a["ids"][:, hot].T),
        "row_numbers_dram": np.arange(P * HOT_CHUNKS, dtype=np.float32).reshape(P, HOT_CHUNKS),
        "dense_dram": np.ascontiguousarray(a["dense_ctx"].T),
        "w1_dram": w1_placed.reshape(P, -1),
        "b1_dram": np.ascontiguousarray(a["b_top1"].reshape(-1, P).T),
        "w2_dram": a["W_top2"],
        "b2_dram": np.ascontiguousarray(a["b_top2"].reshape(-1, P).T),
        "w3_dram": np.ascontiguousarray(a["W_top3"].reshape(-1, P).T),
    }
    nc = bacc.Bacc("TRN2", target_bir_lowering=False, num_devices=1)
    args = [nc.dram_tensor(name, v.shape, mybir.dt.from_np(v.dtype), kind="ExternalInput").ap()
            for name, v in arrays.items()]
    out = nc.dram_tensor("out_dram", (n_batch, 1), F32, kind="ExternalOutput").ap()
    build_tower(nc, *args, out)
    result = run_bass_kernel_spmd(nc, [arrays], core_ids=[0])
    return result.results[0]["out_dram"]
```

```python
from contextlib import ExitStack

import numpy as np

import concourse.bass as bass
from concourse import mybir

F32 = mybir.dt.float32
F32R = mybir.dt.float32r
F16 = mybir.dt.float16
I32 = mybir.dt.int32
U32 = mybir.dt.uint32
ALU = mybir.AluOpType
ACT = mybir.ActivationFunctionType

P = 128
FEATS = 32
HOT = 10
COLD = FEATS - HOT
DIM = 128
HOT_CHUNKS = 8
HOT_BUFS = 2
QUAD = 32
NQ = P // QUAD
BANK = 512
BLOCK = NQ * BANK // FEATS
GROUPS = BLOCK // NQ
WARM_UP = 14
TILL_COPIED = 2
TILL_PAIRS = 5
LOW_AT = 2
LAST_PARTS = 2
PER_GATHER = P // BLOCK
GATHERS = COLD // PER_GATHER
SET_SIZES = [3, 3, 3, 2]
SETS = len(SET_SIZES)
SET_AT = [sum(SET_SIZES[:n]) for n in range(SETS + 1)]
HALF = QUAD // 2
COL_CHUNKS = FEATS // NQ
STAGED = 2
CHUNKS = COL_CHUNKS - STAGED
SOON_CHUNKS = range(CHUNKS - STAGED)
LATE_CHUNKS = range(CHUNKS - STAGED, CHUNKS)
assert (CHUNKS - STAGED) * NQ == HALF
UNIT = 2 * BLOCK
BLOCKS = 4
TURN = BLOCKS * BLOCK
UNITS = TURN // UNIT
ALL_SETS = range(SETS)
SOON_SETS = range(SETS // 2)
LATE_SETS = range(SETS // 2, SETS)
assert UNITS == 2
assert SET_AT[SETS] == GATHERS and max(SET_SIZES) * P <= BANK and SETS % 2 == 0


def build_tower(nc, table, ids_firsts, hot_tables, hot_ids, row_numbers, dense, w1, w2, biases_w3, out):
    n_batch = out.shape[0]
    n_dense = dense.shape[0]
    n_h1, n_h2 = w2.shape
    M1, M2 = n_h1 // P, n_h2 // P
    assert n_dense == HALF
    turns = n_batch // TURN
    n_gathers = ids_firsts.shape[1] // 2
    hot_turns = HOT // HOT_BUFS

    with ExitStack() as ctx:
        def sb(name, shape, dt=F32):
            return ctx.enter_context(nc.sbuf_tensor(name, shape, dt))

        def psum(name, shape):
            return ctx.enter_context(nc.psum_tensor(name, shape, F32))

        def sem(name):
            return ctx.enter_context(nc.semaphore(name))

        ids_firsts_sb = sb("ids_firsts_sb", [P, 2, n_gathers], I32)
        all_rows = sb("all_rows", [P, n_gathers], I32)
        row_idx = sb("row_idx", [P, BLOCKS, GATHERS], I32)
        rows = sb("rows", [P, BLOCKS * GATHERS, DIM])
        identity = sb("identity", [P, P])
        zero = sb("zero", [P, 1])
        unused = sb("unused", [P, 1])
        distance = sb("distance", [P, n_batch])
        numbers_sb = sb("numbers_sb", [P, HOT_CHUNKS + 1])
        hot_id = [sb(f"hot_id{w}", [P, n_batch], I32) for w in range(HOT_BUFS)]
        hot_id_16 = sb("hot_id_16", [P, HOT, n_batch], F16)
        whole = sb("whole", [P, HOT, HOT_CHUNKS, DIM])
        high = [sb(f"high{i}", [P, HOT_CHUNKS, DIM], F32R) for i in range(HOT_BUFS)]
        low = [sb(f"low{i}", [P, HOT_CHUNKS, DIM], F32R) for i in range(HOT_BUFS)]
        one_hot = [sb(f"one_hot{i}", [P, HOT_CHUNKS, n_batch], F32R) for i in range(HOT_BUFS)]
        hot_t = sb("hot_t", [P, HOT, n_batch])
        emb_t = [sb(f"emb_t{i}", [P, BLOCK, FEATS]) for i in range(2)]
        pairs = sb("pairs", [P, COL_CHUNKS, n_batch])
        w1_sb = sb("w1_sb", [P, CHUNKS, n_h1])
        w2_sb = sb("w2_sb", [P, M1, n_h2])
        biases_w3_sb = sb("biases_w3_sb", [P, M1 + 2 * M2])
        b1_sb = biases_w3_sb[:, 0:M1]
        b2_sb = biases_w3_sb[:, M1:M1 + M2]
        w3_sb = biases_w3_sb[:, M1 + M2:]
        h1 = sb("h1", [P, M1, UNIT])
        h2 = sb("h2", [P, M2, UNIT])
        y = sb("y", [1, n_batch])

        turned = [psum(f"turned{n}", [P, BANK // BLOCK, BLOCK]) for n in range(SETS)]
        gram = [psum(f"gram{i}", [P, GROUPS, FEATS]) for i in range(2)]
        h1_ps = psum("h1_ps", [P, M1, UNIT])
        h2y_ps = psum("h2y_ps", [P, BANK // UNIT, UNIT])
        h2_ps = h2y_ps[:, 0:M2, :]
        y_ps = h2y_ps[0:1, M2, :]
        hot_ps = [bank[:].rearrange("p m s -> p (m s)") for bank in (h1_ps, h2y_ps)]
        busy_ps = h1_ps[:, 0, :]
        unit_h1_ps = [h1_ps[:, m, :] for m in range(M1)]
        last_h1_ps = [turned[m][:, 0:UNIT // BLOCK, :].rearrange("p f s -> p (f s)") for m in range(M1)]
        last_h2_ps = [gram[m][:, 0:UNIT // FEATS, :].rearrange("p g f -> p (g f)") for m in range(M2)]

        def sets_of_table(w):
            return range(w * SETS // HOT_BUFS, (w + 1) * SETS // HOT_BUFS)

        def hot_table(i):
            return whole[:, bass.ds(i, 1), :, :].rearrange("p i c d -> p (i c) d")

        ids_in = sem("ids_in")
        numbers_in = sem("numbers_in")
        dense_in = sem("dense_in")
        weights_in = sem("weights_in")
        n_weights = 3
        table_in = [sem(f"table_in{w}") for w in range(HOT_BUFS)]
        hot_id_in = [sem(f"hot_id_in{w}") for w in range(HOT_BUFS)]
        ids_16_ready = sem("ids_16_ready")
        one_hot_ready = sem("one_hot_ready")
        high_ready = sem("high_ready")
        low_ready = sem("low_ready")
        hot_done = sem("hot_done")
        hot_banks = sem("hot_banks")
        zeroed = sem("zeroed")
        zero_ready = sem("zero_ready")
        last_h1_done = sem("last_h1_done")
        last_h1_ready = sem("last_h1_ready")
        last_h2_done = sem("last_h2_done")
        last_h2_low = sem("last_h2_low")
        last_h2_high = sem("last_h2_high")
        distance_ready = sem("distance_ready")
        last_chunk_ready = sem("last_chunk_ready")
        identity_ready = sem("identity_ready")
        rows_known = sem("rows_known")
        idx_ready = sem("idx_ready")
        gather_waits = sem("gather_waits")
        gathered = [sem(f"gathered{i}") for i in range(BLOCKS * SETS)]
        transposed = sem("transposed")
        copied = [sem("even_copied"), sem("odd_copied")]
        hot_placed = sem("hot_placed")
        gram_ready = sem("gram_ready")
        pairs_low = sem("pairs_low")
        pairs_high = sem("pairs_high")
        packed = sem("packed")
        h1_done = sem("h1_done")
        h1_ready = sem("h1_ready")
        h2_done = sem("h2_done")
        h2_ready = sem("h2_ready")
        y_done = sem("y_done")
        y_ready = sem("y_ready")
        stored = sem("stored")

        block = ctx.enter_context(nc.Block())

        @block.sync
        def _(sp):
            sp.dma_start(ids_firsts_sb[:], ids_firsts.rearrange("p (a n) -> p a n", a=2)).then_inc(ids_in, 16)

            def load_ids(i, w):
                sp.dma_start(hot_id[w][:], hot_ids[bass.ds(i, 1), :].broadcast_to([P, n_batch])
                             ).then_inc(hot_id_in[w], 16)

            def load_table(i, w):
                sp.dma_start(hot_table(i), hot_tables[bass.ds(i, 1), :, :, :].rearrange("i p c d -> (i p) c d")
                             ).then_inc(table_in[w], 16)

            for w in range(HOT_BUFS):
                load_ids(w, w)
                load_table(w, w)
            with sp.Fori(1, hot_turns) as j:
                for w in range(HOT_BUFS):
                    sp.wait_ge(table_in[w], j * 16)
                    load_table(j * HOT_BUFS + w, w)
                    sp.wait_ge(ids_16_ready, j * HOT_BUFS + (w + 1 - HOT_BUFS))
                    load_ids(j * HOT_BUFS + w, w)
            sp.dma_start(w1_sb[:], w1.rearrange("p (c n) -> p c n", c=CHUNKS)).then_inc(weights_in, 16)
            sp.dma_start(w2_sb[:], w2.rearrange("(k p) n -> p k n", p=P)).then_inc(weights_in, 16)

            def pack(t):
                for v in range(UNITS):
                    sp.wait_ge(dense_in, 16)
                    samples = bass.ds(t * TURN + v * UNIT, UNIT)
                    for q in range(NQ):
                        sp.wait_ge(pairs_low, t * (BLOCKS * NQ) + (2 * v + 1) * NQ + (q + 1))
                        sp.wait_ge(pairs_high, t * (BLOCKS * NQ) + (2 * v + 1) * NQ + (q + 1))
                        sp.dma_start(pairs[q * QUAD:q * QUAD + HALF, CHUNKS - STAGED:CHUNKS, samples],
                                     pairs[q * QUAD + HALF:(q + 1) * QUAD, CHUNKS:COL_CHUNKS, samples]
                                     ).then_inc(packed, 16)

            with sp.Fori(0, turns) as t:
                pack(t)
            sp.wait_ge(y_ready, n_batch // UNIT)
            sp.dma_start(out.rearrange("b o -> o b"), y[:]).then_inc(stored, 16)
            sp.wait_ge(stored, 16)

        @block.gpsimd
        def _(pool):
            nc.gpsimd.memset(identity[:], 0.0).then_inc(zeroed, 1)
            pool.wait_ge(zeroed, 1)
            nc.gpsimd.affine_select(out=identity[:], in_=identity[:], compare_op=ALU.not_equal, fill=1.0, base=0,
                                    pattern=[[-1, P]], channel_multiplier=1).then_inc(identity_ready, 1)

            def wait(signal, value):
                pool.wait_ge(signal, value)
                pool.sem_inc(gather_waits, 1)

            def gather_turn(t, first):
                for u in range(BLOCKS):
                    wait(idx_ready, t * BLOCKS + (u + 1))
                    for n in range(SETS):
                        if not first:
                            wait(transposed, t * (BLOCKS * SETS) + ((u - BLOCKS) * SETS + n + 1))
                        for k in range(SET_AT[n], SET_AT[n + 1]):
                            pool.indirect_dma_start(
                                rows[:, u * GATHERS + k, :], None, table,
                                bass.IndirectOffsetOnAxis(row_idx[:, u, k:k + 1].bitcast(U32), 0),
                            ).then_inc(gathered[u * SETS + n], 16)

            gather_turn(0, True)
            with pool.Fori(1, turns) as t:
                gather_turn(t, False)

        def copy_sets(eng, copy, parities, t, u, sets=range(SETS)):
            for n in sets:
                if n % 2 not in parities:
                    continue
                eng.wait_ge(transposed, t * (BLOCKS * SETS) + (u * SETS + n + 1))
                first, end = HOT + SET_AT[n] * PER_GATHER, HOT + SET_AT[n + 1] * PER_GATHER
                copy(emb_t[u % 2][:, :, first:end].rearrange("p s f -> p f s"),
                     turned[n][:, 0:end - first, :]).then_inc(copied[n % 2], 1)

        def move_pairs(eng, copy, samples, t, u, done, part=0, parts=1):
            eng.wait_ge(gram_ready, t * BLOCKS + (u + part + 1))
            start = t * TURN + u * BLOCK + part * (BLOCK // parts)
            groups = slice(part * GROUPS // parts, (part + 1) * GROUPS // parts)
            for q in range(NQ):
                for s in samples:
                    c1 = COL_CHUNKS - 1 if q == NQ - 1 else COL_CHUNKS
                    src = gram[(u + part) % 2][s * QUAD:(s + 1) * QUAD, groups, :].rearrange("p g (c q) -> p c g q", q=NQ)
                    dst = pairs[q * QUAD:(q + 1) * QUAD, 0:c1, bass.ds(start, BLOCK // parts)]
                    dst = dst.rearrange("p c (g s) -> p c g s", s=NQ)
                    last = copy(dst[:, :, :, s], src[:, 0:c1, :, q])
                if part == parts - 1:
                    last.then_inc(done, 1)

        @block.vector
        def _(dve):
            nc.vector.memset(zero[:], 0.0).then_inc(zero_ready, 1)
            dve.wait_ge(ids_in, 16)
            nc.vector.tensor_tensor(all_rows[:], ids_firsts_sb[:, 0, :], ids_firsts_sb[:, 1, :], ALU.add).then_inc(rows_known, 1)
            dve.wait_ge(rows_known, 1)

            def number_rows(t, u):
                nc.vector.tensor_copy(row_idx[:, u, :], all_rows[:, bass.ds(t * (BLOCKS * GATHERS) + u * GATHERS, GATHERS)]
                                      ).then_inc(idx_ready, 1)

            for u in range(BLOCKS):
                number_rows(0, u)

            dve.wait_ge(numbers_in, 16)

            def hot_turn(j, last):
                for w in range(HOT_BUFS):
                    i = j * HOT_BUFS + w
                    dve.wait_ge(hot_banks, i + 1)
                    dve.wait_ge(ids_16_ready, i + 1)
                    low_at = LOW_AT if last and w == HOT_BUFS - 1 else HOT_CHUNKS - 1
                    for c in range(HOT_CHUNKS):
                        if c == low_at:
                            dve.wait_ge(high_ready, i + 1)
                            nc.vector.tensor_tensor(low[w][:], hot_table(i), high[w][:].bitcast(F32), ALU.subtract
                                                    ).then_inc(low_ready, 1)
                        if c < HOT_CHUNKS - 1:
                            nc.vector.tensor_scalar(
                                one_hot[w][:, c, :], hot_id_16[:, bass.ds(i, 1), :].rearrange("p h b -> p (h b)"),
                                numbers_sb[:, c:c + 1], None, ALU.is_equal).then_inc(one_hot_ready, 1)

            with dve.Fori(0, hot_turns - 1) as j:
                hot_turn(j, False)
            hot_turn(hot_turns - 1, True)

            def copy_even(t, u, sets=ALL_SETS):
                copy_sets(dve, nc.vector.tensor_copy, (0,), t, u, sets)

            def move_block(t, u, parts=1):
                for part in range(parts):
                    move_pairs(dve, nc.vector.tensor_copy, range(NQ // 2, NQ), t, u, pairs_high, part, parts)

            def number_next(t, u):
                dve.wait_ge(transposed, t * (BLOCKS * SETS) + (u + 1) * SETS)
                number_rows(t + 1, u)

            def turn(t, first, last):
                if not last:
                    number_next(t, 0)
                    number_next(t, 1)
                for v in range(UNITS):
                    if first and v == 0:
                        move_block(t, 0)
                        copy_even(t, 2)
                        move_block(t, 1)
                        number_next(t, 2)
                        copy_even(t, 3)
                        number_next(t, 3)
                    else:
                        last_unit = last and v == UNITS - 1
                        move_block(t, 2 * v)
                        if last_unit:
                            copy_even(t, 2 * v + 1, LATE_SETS)
                        move_block(t, 2 * v + 1, LAST_PARTS if last_unit else 1)
                        if not last_unit:
                            copy_even(t, 2 * v + 2)
                            if v == 0 and not last:
                                number_next(t, 2 * v + 2)
                            copy_even(t, 2 * v + 3, SOON_SETS if last and v == UNITS - 2 else ALL_SETS)
                            if v == 0 and not last:
                                number_next(t, 2 * v + 3)

            turn(0, True, False)
            if turns > 2:
                with dve.Fori(1, turns - 1) as t:
                    turn(t, False, False)
            turn(turns - 1, False, True)
            dve.wait_ge(weights_in, 16 * n_weights)
            for m in range(1, M2):
                dve.wait_ge(last_h2_done, m + 1)
                dve.wait_ge(y_ready, n_batch // UNIT - 1)
                nc.vector.tensor_scalar(h2[:, m, :], last_h2_ps[m], b2_sb[:, m:m + 1], 0.0, ALU.add, ALU.max
                                        ).then_inc(last_h2_high, 1)

        @block.scalar
        def _(act):
            act.dma_start(numbers_sb[:], row_numbers).then_inc(numbers_in, 16)
            act.wait_ge(zero_ready, 1)
            nc.scalar.activation(unused[:], zero[:], ACT.Relu)

            def convert_ids(j, w):
                act.wait_ge(hot_id_in[w], j * 16 + 16)
                i = bass.ds(j * HOT_BUFS + w, 1)
                nc.scalar.copy(hot_id_16[:, i, :].rearrange("p h b -> p (h b)"), hot_id[w][:]).then_inc(ids_16_ready, 1)

            def round_high(j, w):
                act.wait_ge(hot_banks, j * HOT_BUFS + (w + 1))
                act.wait_ge(table_in[w], j * 16 + 16)
                act.wait_ge(ids_16_ready, j * HOT_BUFS + (w + 1))
                nc.scalar.copy(high[w][:], hot_table(j * HOT_BUFS + w)).then_inc(high_ready, 1)

            def last_chunk(j, w):
                i = j * HOT_BUFS + w
                nc.scalar.activation(distance[:], hot_id_16[:, bass.ds(i, 1), :].rearrange("p h b -> p (h b)"),
                                     ACT.Square, bias=numbers_sb[:, HOT_CHUNKS:]).then_inc(distance_ready, 1)
                act.wait_ge(distance_ready, i + 1)
                nc.scalar.activation(one_hot[w][:, HOT_CHUNKS - 1, :], distance[:], ACT.Relu, bias=1.0,
                                     scale=-1.0).then_inc(last_chunk_ready, 1)

            act.wait_ge(numbers_in, 16)
            for w in range(HOT_BUFS):
                convert_ids(0, w)
                round_high(0, w)
                last_chunk(0, w)

            act.dma_start(biases_w3_sb[:], biases_w3).then_inc(weights_in, 16)
            act.dma_start(pairs[P - HALF:P, COL_CHUNKS - 1, :], dense).then_inc(dense_in, 16)

            def hot_turn(j, last, early_block=None):
                for w in range(HOT_BUFS):
                    if not last:
                        convert_ids(j + 1, w)
                    if early_block is not None:
                        copy_sets(act, nc.scalar.copy, (0, 1), 0, early_block, sets_of_table(w))
                    act.wait_ge(hot_done, j * HOT_BUFS + (w + 1))
                    nc.scalar.copy(hot_t[:, bass.ds(j * HOT_BUFS + w, 1), :].rearrange("p h b -> p (h b)"),
                                   hot_ps[w]).then_inc(hot_banks, 1)
                    if not last:
                        round_high(j + 1, w)
                        last_chunk(j + 1, w)

            with act.Fori(0, hot_turns - 3) as j:
                hot_turn(j, False)
            hot_turn(hot_turns - 3, False, 0)
            hot_turn(hot_turns - 2, False, 1)
            hot_turn(hot_turns - 1, True)
            act.wait_ge(hot_banks, HOT_BUFS + HOT)
            act.wait_ge(weights_in, 16 * n_weights)

            def fill_block(t, u):
                nc.scalar.copy(emb_t[u % 2][:, :, 0:HOT].rearrange("p s f -> p f s"),
                               hot_t[:, :, bass.ds(t * TURN + u * BLOCK, BLOCK)]).then_inc(hot_placed, 1)

            def copy_odd(t, u, sets=ALL_SETS):
                copy_sets(act, nc.scalar.copy, (1,), t, u, sets)

            def move_block(t, u, parts=1):
                for part in range(parts):
                    move_pairs(act, nc.scalar.copy, range(NQ // 2), t, u, pairs_low, part, parts)

            def hidden(dst, src, bias, tiles, t, v, done, ready):
                act.wait_ge(done, t * UNITS + (v + 1))
                for m in range(tiles):
                    last = nc.scalar.activation(dst[:, m, :], src[:, m, :], ACT.Relu, bias=bias[:, m:m + 1])
                last.then_inc(ready, 1)

            def hidden1(t, v):
                hidden(h1, h1_ps, b1_sb, M1, t, v, h1_done, h1_ready)

            def hidden2(t, v):
                hidden(h2, h2_ps, b2_sb, M2, t, v, h2_done, h2_ready)

            def result(t, v):
                act.wait_ge(y_done, t * UNITS + (v + 1))
                nc.scalar.copy(y[:, bass.ds(t * TURN + v * UNIT, UNIT)], y_ps).then_inc(y_ready, 1)

            def turn(t, first, last):
                for v in range(UNITS):
                    before = (t, v - 1) if v else (t - 1, UNITS - 1)
                    first_unit = first and v == 0
                    last_unit = last and v == UNITS - 1
                    move_block(t, 2 * v)
                    if first_unit:
                        copy_odd(t, 2)
                    if last_unit:
                        hidden2(*before)
                        copy_odd(t, 2 * v + 1, LATE_SETS)
                    move_block(t, 2 * v + 1, LAST_PARTS if last_unit else 1)
                    if last_unit:
                        result(*before)
                    else:
                        fill_block(t, 2 * v + 2)
                        if not first_unit:
                            hidden2(*before)
                        fill_block(t, 2 * v + 3)
                        copy_odd(t, 3 if first_unit else 2 * v + 2)
                        hidden1(t, v)
                        if not first_unit:
                            result(*before)
                            copy_odd(t, 2 * v + 3, SOON_SETS if last and v == UNITS - 2 else ALL_SETS)

            fill_block(0, 0)
            fill_block(0, 1)
            turn(0, True, False)
            if turns > 2:
                with act.Fori(1, turns - 1) as t:
                    turn(t, False, False)
            turn(turns - 1, False, True)
            for m in range(M1):
                act.wait_ge(last_h1_done, m + 1)
                nc.scalar.activation(h1[:, m, :], last_h1_ps[m], ACT.Relu, bias=b1_sb[:, m:m + 1]
                                     ).then_inc(last_h1_ready, 1)
            act.wait_ge(last_h2_done, 1)
            nc.scalar.activation(h2[:, 0, :], last_h2_ps[0], ACT.Relu, bias=b2_sb[:, 0:1]).then_inc(last_h2_low, 1)
            result(turns - 1, UNITS - 1)

        @block.tensor
        def _(pe):
            pe.sem_inc(hot_banks, HOT_BUFS)

            def keep_busy(steps):
                for _ in range(steps):
                    nc.tensor.matmul(busy_ps, identity[:], identity[:], start=True, stop=True)

            pe.wait_ge(identity_ready, 1)
            keep_busy(WARM_UP)

            def transpose_block(t, u, sets=ALL_SETS, first=False):
                for n in sets:
                    turn_on, place = divmod(u, BLOCKS)
                    pe.wait_ge(gathered[place * SETS + n], (t + turn_on) * (16 * SET_SIZES[n]) + 16 * SET_SIZES[n])
                    if not first:
                        pe.wait_ge(copied[n % 2], t * (BLOCKS * SETS // 2) + ((u - 1) * SETS // 2 + n // 2 + 1))
                    for k in range(SET_SIZES[n]):
                        last = nc.tensor.transpose(
                            turned[n][:, k * PER_GATHER:(k + 1) * PER_GATHER, :],
                            rows[:, place * GATHERS + SET_AT[n] + k, :], identity[:])
                    last.then_inc(transposed, 1)

            def hot_turn(j, early_block=None, last=False):
                for w in range(HOT_BUFS):
                    i = j * HOT_BUFS + w
                    if early_block is not None:
                        transpose_block(0, early_block, sets_of_table(w), first=(early_block == 0))
                    pe.wait_ge(hot_banks, i + 1)
                    parts = [(high[w], high_ready), (low[w], low_ready)]
                    alone = LOW_AT if last and w == HOT_BUFS - 1 else HOT_CHUNKS
                    steps = [(n, c) for n in range(len(parts)) for c in range(alone)]
                    steps += [(n, c) for c in range(alone, HOT_CHUNKS) for n in range(len(parts))]
                    for n, c in steps:
                        part, ready = parts[n]
                        if c == 0:
                            pe.wait_ge(ready, i + 1)
                        if n == 0:
                            if c < HOT_CHUNKS - 1:
                                pe.wait_ge(one_hot_ready, i * (HOT_CHUNKS - 1) + (c + 1))
                            else:
                                pe.wait_ge(last_chunk_ready, i + 1)
                        product = nc.tensor.matmul(hot_ps[w], part[:, c, :], one_hot[w][:, c, :],
                                                   start=((n, c) == steps[0]), stop=((n, c) == steps[-1]))
                    product.then_inc(hot_done, 1)

            def gram_block(t, u, parts=1):
                sets = (u + 1) * SETS // 2
                pe.wait_ge(copied[0], t * (BLOCKS * SETS // 2) + sets)
                pe.wait_ge(copied[1], t * (BLOCKS * SETS // 2) + sets)
                pe.wait_ge(hot_placed, t * BLOCKS + (u + 1))
                for part in range(parts):
                    if part:
                        pe.wait_ge(pairs_low, (t * BLOCKS + u) * NQ)
                        pe.wait_ge(pairs_high, (t * BLOCKS + u) * NQ)
                    for g in range(part * GROUPS // parts, (part + 1) * GROUPS // parts):
                        for s in range(NQ):
                            x = emb_t[u % 2][:, g * NQ + s, :]
                            last = nc.tensor.matmul(gram[(u + part) % 2][s * QUAD:(s + 1) * QUAD, g, :], x, x,
                                                    start=True, stop=True)
                    last.then_inc(gram_ready, 1)

            def layer1(t, v, sums, meanwhile, tile_done=None):
                pe.wait_ge(weights_in, 16 * n_weights)
                pe.wait_ge(pairs_low, (t * BLOCKS + (2 * v + 2)) * NQ)
                pe.wait_ge(pairs_high, (t * BLOCKS + (2 * v + 2)) * NQ)
                banks = 1 if tile_done is None else M1

                def product(m, c):
                    return nc.tensor.matmul(sums[m], w1_sb[:, c, m * P:(m + 1) * P],
                                            pairs[:, c, bass.ds(t * TURN + v * UNIT, UNIT)],
                                            start=(c == 0 and m < banks), stop=(c == CHUNKS - 1),
                                            skip_group_check=True)

                for m in range(M1):
                    for c in SOON_CHUNKS:
                        product(m, c)
                meanwhile()
                pe.wait_ge(packed, (t * UNITS + (v + 1)) * (16 * NQ))
                for m in range(M1):
                    for c in LATE_CHUNKS:
                        last = product(m, c)
                    if tile_done is not None:
                        last.then_inc(tile_done, 1)
                if tile_done is None:
                    last.then_inc(h1_done, 1)

            def layer2(t, v, first=False):
                pe.wait_ge(h1_ready, t * UNITS + (v + 1))
                if not first:
                    pe.wait_ge(y_ready, t * UNITS + v)
                for m in range(M2):
                    for k in range(M1):
                        last = nc.tensor.matmul(h2_ps[:, m, :], w2_sb[:, k, m * P:(m + 1) * P], h1[:, k, :],
                                                start=(k == 0), stop=(k == M1 - 1))
                last.then_inc(h2_done, 1)

            def layer3(t, v):
                pe.wait_ge(h2_ready, t * UNITS + (v + 1))
                for k in range(M2):
                    last = nc.tensor.matmul(y_ps, w3_sb[:, k:k + 1], h2[:, k, :],
                                            start=(k == 0), stop=(k == M2 - 1))
                last.then_inc(y_done, 1)

            def turn(t, first, last):
                for v in range(UNITS):
                    before = (t, v - 1) if v else (t - 1, UNITS - 1)
                    first_unit = first and v == 0
                    last_unit = last and v == UNITS - 1
                    if first_unit:
                        transpose_block(t, 2)
                    gram_block(t, 2 * v)
                    if last_unit:
                        layer2(*before)
                        transpose_block(t, 2 * v + 1, LATE_SETS)
                        keep_busy(TILL_COPIED)
                    gram_block(t, 2 * v + 1, LAST_PARTS if last_unit else 1)
                    if first_unit:
                        layer1(t, v, unit_h1_ps, lambda: transpose_block(t, 3))
                    elif not last_unit:
                        layer2(*before, first=first)
                        layer1(t, v, unit_h1_ps, lambda: transpose_block(t, 2 * v + 2))
                        layer3(*before)
                        transpose_block(t, 2 * v + 3, SOON_SETS if last and v == UNITS - 2 else ALL_SETS)

            with pe.Fori(0, hot_turns - 3) as j:
                hot_turn(j)
            hot_turn(hot_turns - 3, early_block=0)
            hot_turn(hot_turns - 2, early_block=1)
            hot_turn(hot_turns - 1, last=True)
            turn(0, True, False)
            if turns > 2:
                with pe.Fori(1, turns - 1) as t:
                    turn(t, False, False)
            turn(turns - 1, False, True)

            keep_busy(TILL_PAIRS)
            layer1(turns - 1, UNITS - 1, last_h1_ps, lambda: layer3(turns - 1, UNITS - 2), tile_done=last_h1_done)
            for k in range(M1):
                pe.wait_ge(last_h1_ready, k + 1)
                for m in range(M2):
                    last = nc.tensor.matmul(last_h2_ps[m], w2_sb[:, k, m * P:(m + 1) * P], h1[:, k, :],
                                            start=(k == 0), stop=(k == M1 - 1))
                    if k == M1 - 1:
                        last.then_inc(last_h2_done, 1)
            for k in range(M2):
                pe.wait_ge(last_h2_high if k else last_h2_low, max(k, 1))
                last = nc.tensor.matmul(y_ps, w3_sb[:, k:k + 1], h2[:, k, :], start=(k == 0), stop=(k == M2 - 1))
            last.then_inc(y_done, 1)


def kernel(**inputs):
    import concourse.bacc as bacc
    from concourse.bass_utils import run_bass_kernel_spmd

    a = {name: np.asarray(value) for name, value in inputs.items()}
    tables = [a[f"tbl_{f}"] for f in range(FEATS)]
    n_batch = a["ids"].shape[0]
    blocks = n_batch // BLOCK

    small = [f for f in range(FEATS) if tables[f].shape[0] <= 1000]
    hot = small[-HOT:]
    cold = [f for f in range(FEATS) if f not in hot]
    slots = np.array(hot + cold)

    first_row = np.cumsum([0] + [tables[f].shape[0] for f in cold[:-1]]).astype(np.int32)
    by_gather = (PER_GATHER, BLOCK, blocks, GATHERS)
    ids = a["ids"][:, cold].reshape(blocks, BLOCK, GATHERS, PER_GATHER).transpose(3, 1, 0, 2)
    first = np.broadcast_to(first_row.reshape(GATHERS, PER_GATHER).T[:, None, None, :], by_gather)

    hot_tables = np.zeros((HOT, HOT_CHUNKS * P, DIM), tables[0].dtype)
    for n, f in enumerate(hot):
        hot_tables[n, :tables[f].shape[0]] = tables[f]

    w1 = a["W_top1"]
    i, j = np.triu_indices(FEATS, k=1)
    n_pairs = len(i)
    row_of = np.zeros((FEATS, FEATS), np.int64)
    row_of[i, j] = row_of[j, i] = np.arange(n_pairs)
    staged = i // NQ >= CHUNKS
    w1_placed = np.zeros((NQ, QUAD, CHUNKS, w1.shape[1]), w1.dtype)
    w1_placed[i % NQ, np.where(staged, j - HALF, j), np.where(staged, i // NQ - STAGED, i // NQ)] = \
        w1[row_of[slots[i], slots[j]]]
    w1_placed[NQ - 1, :HALF, CHUNKS - 1] = w1[n_pairs:]

    row_numbers = np.arange(P * HOT_CHUNKS, dtype=np.float32).reshape(P, HOT_CHUNKS)
    row_numbers = np.concatenate([row_numbers, -row_numbers[:, -1:]], axis=1)

    arrays = {
        "table_dram": np.concatenate([tables[f] for f in cold]),
        "ids_firsts_dram": np.concatenate([ids.reshape(P, -1), first.reshape(P, -1)], axis=1),
        "hot_tables_dram": hot_tables.reshape(HOT, P, HOT_CHUNKS, DIM),
        "hot_ids_dram": np.ascontiguousarray(a["ids"][:, hot].T),
        "row_numbers_dram": row_numbers,
        "dense_dram": np.ascontiguousarray(a["dense_ctx"].T),
        "w1_dram": w1_placed.reshape(P, -1),
        "w2_dram": a["W_top2"],
        "biases_w3_dram": np.concatenate([a[name].reshape(-1, P).T for name in ("b_top1", "b_top2", "W_top3")], axis=1),
    }
    nc = bacc.Bacc("TRN2", target_bir_lowering=False, num_devices=1)
    args = [nc.dram_tensor(name, v.shape, mybir.dt.from_np(v.dtype), kind="ExternalInput").ap()
            for name, v in arrays.items()]
    out = nc.dram_tensor("out_dram", (n_batch, 1), F32, kind="ExternalOutput").ap()
    build_tower(nc, *args, out)
    result = run_bass_kernel_spmd(nc, [arrays], core_ids=[0])
    return result.results[0]["out_dram"]
```
